# Optimizing a Trainium2 kernel written in Bass

```python
import numpy as np
import jax
import jax.numpy as jnp

def _softmax(x, axis=-1):
    return jax.nn.softmax(x, axis=axis)

def _gelu(x):
    return jax.nn.gelu(x, approximate=True)

def _silu(x):
    return jax.nn.silu(x)

def _sigmoid(x):
    return jax.nn.sigmoid(x)

def _layernorm(x, axis=-1, eps=1e-05):
    m = jnp.mean(x, axis=axis, keepdims=True)
    v = jnp.var(x, axis=axis, keepdims=True)
    return (x - m) / jnp.sqrt(v + eps)

def _scatter_add(tgt, idx, src, axis=0):
    return tgt.at[idx].add(src)

def _segment_sum(src, seg, n):
    return jax.ops.segment_sum(src, seg, n)
kernel_name = 'mk_adj_resnorm_d1_adj_r2_01b828'

def setup_inputs(seed: int=0):
    np.random.seed(seed)
    _w = jnp.asarray

    def _rec_inputs():
        import jax
        import jax.numpy as jnp
        _gk = jax.random.key(seed)
        x = -0.0005207 + 1.001 * jax.random.normal(jax.random.fold_in(_gk, 1), (8192, 128), jnp.float32)
        _a = jax.random.bernoulli(jax.random.fold_in(_gk, 2), 0.000488281, (8192, 8192))
        _a = jnp.logical_or(_a, jnp.eye(8192, dtype=bool))
        _af = _a.astype(jnp.float32)
        _af = _af * jax.random.uniform(jax.random.fold_in(_gk, 3), (8192, 8192), jnp.float32, 0.05, 1)
        adj = _af
        return (x, adj)
    x, adj = _rec_inputs()

    def _L0_gnn_setup():
        import jax, jax.numpy as jnp
        import numpy as np
        N, IN_C, OUT_C = (4096, 128, 128)
        key = jax.random.key(seed)
        k1, k2, k3 = jax.random.split(key, 3)
        x = jax.random.normal(k1, (N, IN_C), dtype=jnp.float32)
        adj = jax.random.uniform(k2, (N, N), dtype=jnp.float32)
        limit = float(np.sqrt(6.0 / (IN_C + OUT_C)))
        weight = jax.random.uniform(k3, (IN_C, OUT_C), dtype=jnp.float32, minval=-limit, maxval=limit)
        bias = jnp.zeros((OUT_C,), dtype=jnp.float32)
        return {'x': x, 'adj': adj, 'weight': weight, 'bias': bias}
    _L0_gnn_all = _L0_gnn_setup()
    _L0_gnn_in = {k: v for k, v in _L0_gnn_all.items() if k in ('weight', 'bias')}
    del _L0_gnn_all
    return {'x': x, 'adj': adj, 'L0_gnn_weight': _L0_gnn_in['weight'], 'L0_gnn_bias': _L0_gnn_in['bias']}

def reference(x, adj, L0_gnn_weight, L0_gnn_bias):
    import jax
    import jax.numpy as jnp

    def _L0_gnn_ref(x, adj, weight, bias):
        import jax, jax.numpy as jnp
        import numpy as np
        N, IN_C, OUT_C = (4096, 128, 128)
        deg = jnp.sum(adj, axis=1)
        d = deg ** (-0.5)
        d = jnp.where(jnp.isinf(d), 0.0, d)
        adj_norm = d[:, None] * adj * d[None, :]
        support = x @ weight
        out = adj_norm @ support + bias
        return out
    x = _layernorm(x + _L0_gnn_ref(x, adj, L0_gnn_weight, L0_gnn_bias), axis=-1)
    return x

_drawn_inputs = setup_inputs


def setup_inputs(seed=0):
    import zlib

    import numpy as np

    out = dict(_drawn_inputs(seed))
    spreads = {'L0_gnn_bias': (0.0, 0.1)}
    factors = {}
    for name, (base, spread) in spreads.items():
        noise = np.random.default_rng([zlib.crc32(name.encode()), seed]).standard_normal(out[name].shape)
        drawn = base * np.exp(spread * noise) if base else spread * noise
        out[name] = jnp.asarray(drawn.astype(out[name].dtype))
    for name, factor in factors.items():
        out[name] = (out[name] * factor).astype(out[name].dtype)
    return out
```

```python
import concourse.bass as bass
from concourse import mybir
from contextlib import ExitStack


def normalized_adjacency_layernorm(nc, adj_t, x, x_t, weight, bias, out):
    f32 = mybir.dt.float32
    ALU = mybir.AluOpType
    ACT = mybir.ActivationFunctionType

    P = 128
    N, C = x.shape
    TILE = adj_t.shape[-1]
    KB = TILE // P
    NT = N // TILE
    CELLS = KB * TILE
    EPS = 1e-5
    F32_MAX = 3.4028234e38

    BAND = 3
    RING = 6
    LEAD = 4
    BANKS = 5
    PARKED = NT - 1 - BAND

    def load_order(row):
        lead = min(LEAD, row)
        only_summed = list(range(NT - 1, row + BAND, -1))
        waiting = list(range(min(row + BAND, NT - 1), row - 1, -1))
        at_once = list(range(row - 1, -1, -1))
        return only_summed + at_once[:lead] + waiting + at_once[lead:]

    def multiplied_at_once(row):
        return range(row - 1, -1, -1)

    def waited_for(col):
        return range(max(0, col - BAND), col + 1)

    def adds_through(row, position):
        return row * (NT - 1) + max(position, 1)

    band_slot = [RING + d * (d + 1) // 2 for d in range(BAND + 1)]
    SLOTS = RING + (BAND + 1) * (BAND + 2) // 2

    TURNS = NT + PARKED
    FIRST_DONE = NT - 1 - BAND

    def row_of(turn):
        return turn if turn < NT else NT + PARKED - 1 - turn

    products = []
    for i in range(NT):
        products += [(i, j) for j in multiplied_at_once(i)]
        products += [(k, i) for k in waited_for(i)]
    for t in range(NT, TURNS):
        products += [(t, j) for j in range(row_of(t) + BAND + 1, NT)]
    product_no = {p: n for n, p in enumerate(products)}
    first_of = {t: min(n for n, p in enumerate(products) if p[0] == t) for t in range(TURNS)}
    last_of = {t: max(n for n, p in enumerate(products) if p[0] == t) for t in range(TURNS)}

    loads = []
    slot_of, load_count = {}, {}
    uses, free_after = [0] * SLOTS, [(0, 0)] * SLOTS
    passing = 0
    for t in range(TURNS):
        for pos, j in enumerate(load_order(t) if t < NT else range(row_of(t) + BAND + 1, NT)):
            d = j - t
            if t >= NT:
                slot = (passing - 1) % SLOTS
                passing += 1
            elif 0 <= d <= BAND:
                slot = band_slot[d] + t % (d + 1)
            else:
                slot = passing % RING
                passing += 1
                if t == NT - 1 and j == 0:
                    passing = 0
            uses[slot] += 1
            loads.append((t, j, slot, free_after[slot]))
            slot_of[t, j], load_count[t, j] = slot, uses[slot]
            free_after[slot] = (adds_through(t, pos) if t < NT else 0,
                                product_no[t, j] + 1 if (t, j) in product_no else 0)

    with ExitStack() as ctx:
        def sb(name, shape, dt=f32):
            return ctx.enter_context(nc.sbuf_tensor(name, shape, dt))

        def ps(name, shape):
            return ctx.enter_context(nc.psum_tensor(name, shape, f32))

        def sem(name):
            return ctx.enter_context(nc.semaphore(name))

        tiles = sb("tiles", [P, SLOTS, CELLS])
        scaled = sb("scaled", [P, NT * KB, C])
        parked = sb("parked", [P, PARKED, TILE])
        sums = sb("sums", [P, 2, CELLS])
        xt_in = sb("xt_in", [P, 2, TILE])
        w_in = sb("w_in", [P, C])
        ident = sb("ident", [P, P])
        bias_in = sb("bias_in", [P, C])
        ones = sb("ones", [P, 1])
        minus_half = sb("minus_half", [P, KB])
        zeros = sb("zeros", [P, KB])
        degree = sb("degree", [P, NT, KB])
        d = sb("d", [P, NT, KB])
        is_inf = sb("is_inf", [P, KB], mybir.dt.int32)
        z_sum = sb("z_sum", [P, 2, KB])
        minus_mean = sb("minus_mean", [P, 2, KB])
        square_sum = sb("square_sum", [P, 2, KB])
        variance = sb("variance", [P, 2, KB])
        rstd = sb("rstd", [P, 2, KB])
        shift = sb("shift", [P, 2, KB])
        whole_t = sums[:, 0, 0:2 * TILE].rearrange("p (b i) -> p b i", b=2)
        z = sums[:, 0, 2 * TILE:4 * TILE].rearrange("p (b i c) -> p b i c", b=2, c=C)
        x_in = sums[:, 1, 0:2 * TILE].rearrange("p (b i c) -> p b i c", b=2, c=C)
        squares = sums[:, 1, 2 * TILE:3 * TILE].rearrange("p (i c) -> p i c", c=C)

        acc = [ps(f"acc{b}", [P, TILE]) for b in range(BANKS)]
        degree_ps = ps("degree_ps", [P, 2, KB])
        turned = [ps(f"turned{b}", [P, KB, C]) for b in range(2)]

        tile_loaded = [sem(f"tile_loaded{s}") for s in range(SLOTS)]
        xt_loaded = [sem(f"xt_loaded{b}") for b in range(2)]
        x_loaded = [sem(f"x_loaded{b}") for b in range(2)]
        y_stored = [sem(f"y_stored{b}") for b in range(2)]
        consts_loaded = sem("consts_loaded")
        consts_set = sem("consts_set")
        ident_cleared = sem("ident_cleared")
        ident_ready = sem("ident_ready")
        added = sem("added")
        multiplied = sem("multiplied")
        xw_product = sem("xw_product")
        xw_saved = sem("xw_saved")
        degree_product = sem("degree_product")
        degree_saved = sem("degree_saved")
        powered = sem("powered")
        masked = sem("masked")
        d_ready = sem("d_ready")
        scaled_ready = sem("scaled_ready")
        park_ready = sem("park_ready")
        whole_ready = sem("whole_ready")
        turned_back = sem("turned_back")
        xb_ready = sem("xb_ready")
        z_ready = sem("z_ready")
        mean_ready = sem("mean_ready")
        squared = sem("squared")
        variance_ready = sem("variance_ready")
        rstd_ready = sem("rstd_ready")
        shift_ready = sem("shift_ready")
        y_ready = sem("y_ready")

        block = ctx.enter_context(nc.Block())
        rows_of = x.rearrange("(t k p) c -> t p k c", k=KB, p=P)
        out_rows = out.rearrange("(t k p) c -> t p k c", k=KB, p=P)

        @block.sync
        def _(sp):
            sp.dma_start(w_in[:, :], weight[:, :]).then_inc(consts_loaded, 16)
            sp.dma_start(bias_in[:, :], bias.rearrange("(a c) -> a c", a=1).to_broadcast([P, C])
                         ).then_inc(consts_loaded, 16)
            for n, (t, j, slot, (adds, mults)) in enumerate(loads):
                if t < NT and (n == 0 or loads[n - 1][0] != t):
                    if t >= 2:
                        sp.wait_ge(xw_product, t - 1)
                    sp.dma_start(xt_in[:, t % 2, :], x_t[:, t * TILE:(t + 1) * TILE]
                                 ).then_inc(xt_loaded[t % 2], 16)
                if adds:
                    sp.wait_ge(added, adds)
                if mults:
                    sp.wait_ge(multiplied, mults)
                sp.dma_start(tiles[:, slot, :], adj_t[row_of(t), j]).then_inc(tile_loaded[slot], 16)

        @block.vector
        def _(dve):
            nc.vector.memset(ones[:, :], 1.0)
            nc.vector.memset(minus_half[:, :], -0.5)
            nc.vector.memset(zeros[:, :], 0.0).then_inc(consts_set, 1)

            def degree_guard(i):
                dve.wait_ge(powered, i + 1)
                nc.vector.tensor_scalar(is_inf[:, :], d[:, i, :], F32_MAX, None, ALU.is_gt
                                        ).then_inc(masked, 1)
                dve.wait_ge(masked, i + 1)
                nc.vector.copy_predicated(d[:, i, :], is_inf[:, :], zeros[:, :]).then_inc(d_ready, 1)

            for i in range(NT):
                order = load_order(i)
                for pos in range(1, NT):
                    for j in (order[0:2] if pos == 1 else order[pos:pos + 1]):
                        dve.wait_ge(tile_loaded[slot_of[i, j]], 16 * load_count[i, j])
                    total = sums[:, i % 2, :]
                    before = tiles[:, slot_of[i, order[0]], :]
                    if pos == 1:
                        if i >= 2:
                            dve.wait_ge(degree_product, i - 1)
                    else:
                        before = total
                        dve.wait_ge(added, adds_through(i, pos) - 1)
                    nc.vector.tensor_tensor(total, before, tiles[:, slot_of[i, order[pos]], :],
                                            ALU.add).then_inc(added, 1)
                    if pos == 1 and i >= 1:
                        degree_guard(i - 1)
            degree_guard(NT - 1)

            def whole(e):
                t = FIRST_DONE + e
                dve.wait_ge(multiplied, last_of[t] + 1)
                if e >= 2:
                    dve.wait_ge(turned_back, e - 1)
                if t < NT:
                    nc.vector.tensor_copy(whole_t[:, e % 2, :], acc[t % BANKS][:, :]
                                          ).then_inc(whole_ready, 1)
                else:
                    dve.wait_ge(park_ready, row_of(t) + 1)
                    nc.vector.tensor_tensor(whole_t[:, e % 2, :], acc[t % BANKS][:, :],
                                            parked[:, row_of(t), :], ALU.add).then_inc(whole_ready, 1)

            def residual(e):
                b, r = e % 2, row_of(FIRST_DONE + e)
                dve.wait_ge(x_loaded[b], 16 * (e // 2 + 1))
                if e == 0:
                    dve.wait_ge(consts_loaded, 32)
                nc.vector.tensor_tensor(x_in[:, b], x_in[:, b],
                                        bias_in[:, None, :].to_broadcast([P, KB, C]), ALU.add
                                        ).then_inc(xb_ready, 1)
                dve.wait_ge(xb_ready, e + 1)
                dve.wait_ge(turned_back, e + 1)
                if e >= 2:
                    dve.wait_ge(y_stored[b], 16 * (e // 2))
                for k in range(KB):
                    nc.vector.scalar_tensor_tensor(z[:, b, k, :], turned[b][:, k, :], d[:, r, k:k + 1],
                                                   x_in[:, b, k, :], ALU.mult, ALU.add,
                                                   accum_out=z_sum[:, b, k:k + 1]).then_inc(z_ready, 1)
                dve.wait_ge(z_ready, KB * (e + 1))
                nc.vector.tensor_scalar(minus_mean[:, b, :], z_sum[:, b, :], -1.0 / C, None, ALU.mult
                                        ).then_inc(mean_ready, 1)

            def deviation(e):
                b = e % 2
                dve.wait_ge(squared, KB * (e + 1))
                nc.vector.tensor_scalar(variance[:, b, :], square_sum[:, b, :], 1.0 / C, EPS,
                                        ALU.mult, ALU.add).then_inc(variance_ready, 1)
                dve.wait_ge(rstd_ready, e + 1)
                nc.vector.tensor_tensor(shift[:, b, :], minus_mean[:, b, :], rstd[:, b, :], ALU.mult
                                        ).then_inc(shift_ready, 1)

            whole(0)
            for e in range(NT):
                if e + 1 < NT and e < BAND:
                    whole(e + 1)
                residual(e)
                deviation(e)
                if e + 1 < NT and e >= BAND:
                    whole(e + 1)

        @block.gpsimd
        def _(pool):
            nc.gpsimd.memset(ident[:, :], 0.0).then_inc(ident_cleared, 1)
            pool.wait_ge(ident_cleared, 1)
            nc.gpsimd.affine_select(out=ident[:, :], in_=ident[:, :], compare_op=ALU.not_equal, fill=1.0,
                                    base=0, pattern=[[-1, P]], channel_multiplier=1).then_inc(ident_ready, 1)
            pool.wait_ge(consts_set, 1)
            for i in range(NT):
                pool.wait_ge(degree_saved, i + 1)
                nc.gpsimd.tensor_tensor(d[:, i, :], degree[:, i, :], minus_half[:, :], ALU.pow
                                        ).then_inc(powered, 1)
            for e in range(NT):
                pool.wait_ge(variance_ready, e + 1)
                nc.gpsimd.tensor_tensor(rstd[:, e % 2, :], variance[:, e % 2, :], minus_half[:, :], ALU.pow
                                        ).then_inc(rstd_ready, 1)

        @block.scalar
        def _(act):
            for i in range(NT):
                act.wait_ge(xw_product, i + 1)
                nc.scalar.activation(scaled[:, i * KB:(i + 1) * KB, :], turned[i % 2][:, :, :], ACT.Copy
                                     ).then_inc(xw_saved, 1)
                act.wait_ge(degree_product, i + 1)
                nc.scalar.activation(degree[:, i, :], degree_ps[:, i % 2, :], ACT.Copy).then_inc(degree_saved, 1)
                act.wait_ge(d_ready, i + 1)
                act.wait_ge(xw_saved, i + 1)
                for k in range(KB):
                    nc.scalar.activation(scaled[:, i * KB + k, :], scaled[:, i * KB + k, :], ACT.Copy,
                                         scale=d[:, i, k:k + 1]).then_inc(scaled_ready, 1)
                if BAND <= i < NT - 1:
                    act.wait_ge(multiplied, product_no[i - BAND, i] + 1)
                    nc.scalar.activation(parked[:, i - BAND, :], acc[(i - BAND) % BANKS][:, :], ACT.Copy
                                         ).then_inc(park_ready, 1)
            act.wait_ge(degree_product, NT)
            for e in range(2):
                act.dma_start(x_in[:, e], rows_of[row_of(FIRST_DONE + e)]).then_inc(x_loaded[e], 16)
            for e in range(NT):
                b, r = e % 2, row_of(FIRST_DONE + e)
                act.wait_ge(mean_ready, e + 1)
                for k in range(KB):
                    nc.scalar.activation(squares[:, k, :], z[:, b, k, :], ACT.Square,
                                         bias=minus_mean[:, b, k:k + 1],
                                         accum_out=square_sum[:, b, k:k + 1]).then_inc(squared, 1)
                if e + 2 < NT:
                    act.dma_start(x_in[:, b], rows_of[row_of(FIRST_DONE + e + 2)]).then_inc(x_loaded[b], 16)
                act.wait_ge(squared, KB * (e + 1))
                act.wait_ge(shift_ready, e + 1)
                for k in range(KB):
                    nc.scalar.activation(z[:, b, k, :], z[:, b, k, :], ACT.Identity,
                                         bias=shift[:, b, k:k + 1], scale=rstd[:, b, k:k + 1]
                                         ).then_inc(y_ready, 1)
                act.wait_ge(y_ready, KB * (e + 1))
                act.dma_start(out_rows[r], z[:, b]).then_inc(y_stored[b], 16)
            for b in range(2):
                act.wait_ge(y_stored[b], 16 * (NT // 2))

        @block.tensor
        def _(pe):
            def xw(i):
                pe.wait_ge(xt_loaded[i % 2], 16 * (i // 2 + 1))
                if i == 0:
                    pe.wait_ge(consts_loaded, 32)
                if i >= 2:
                    pe.wait_ge(xw_saved, i - 1)
                for k in range(KB):
                    last = nc.tensor.matmul(turned[i % 2][:, k, :], xt_in[:, i % 2, k * P:(k + 1) * P],
                                            w_in[:, :], start=True, stop=True)
                last.then_inc(xw_product, 1)

            def degrees(i):
                pe.wait_ge(added, (i + 1) * (NT - 1))
                if i == 0:
                    pe.wait_ge(consts_set, 1)
                if i >= 2:
                    pe.wait_ge(degree_saved, i - 1)
                for m in range(KB):
                    for k in range(KB):
                        at = k * TILE + m * P
                        last = nc.tensor.matmul(degree_ps[:, i % 2, m:m + 1], sums[:, i % 2, at:at + P],
                                                ones[:, :], start=(k == 0), stop=(k == KB - 1))
                last.then_inc(degree_product, 1)

            def multiply(t, j):
                n = product_no[t, j]
                pe.wait_ge(tile_loaded[slot_of[t, j]], 16 * load_count[t, j])
                pe.wait_ge(scaled_ready, KB * (j + 1))
                if n == first_of[t] and t >= BANKS:
                    before = t - BANKS
                    if before < FIRST_DONE:
                        pe.wait_ge(park_ready, before + 1)
                    else:
                        pe.wait_ge(whole_ready, before - FIRST_DONE + 1)
                for k in range(KB):
                    last = nc.tensor.matmul(acc[t % BANKS][:, :], scaled[:, j * KB + k, :],
                                            tiles[:, slot_of[t, j], k * TILE:(k + 1) * TILE],
                                            start=(n == first_of[t] and k == 0),
                                            stop=(n == last_of[t] and k == KB - 1))
                last.then_inc(multiplied, 1)

            def turn_back(e):
                pe.wait_ge(whole_ready, e + 1)
                if e >= 2:
                    pe.wait_ge(z_ready, KB * (e - 1))
                else:
                    pe.wait_ge(xw_saved, NT)
                if e == 0:
                    pe.wait_ge(ident_ready, 1)
                for k in range(KB):
                    last = nc.tensor.transpose(turned[e % 2][:, k, :], whole_t[:, e % 2, k * P:(k + 1) * P],
                                               ident[:, :])
                last.then_inc(turned_back, 1)

            for i in range(NT):
                xw(i)
                at_once = list(multiplied_at_once(i))
                held = 2 if i >= LEAD else 0
                for j in at_once[:len(at_once) - held]:
                    multiply(i, j)
                degrees(i)
                for j in at_once[len(at_once) - held:]:
                    multiply(i, j)
                for k in waited_for(i):
                    multiply(k, i)
                    if i == NT - 1 and k > FIRST_DONE:
                        turn_back(k - 1 - FIRST_DONE)
            for t in range(NT, TURNS):
                for m, j in enumerate(range(row_of(t) + BAND + 1, NT)):
                    multiply(t, j)
                    if m == 0:
                        turn_back(t - 1 - FIRST_DONE)
            turn_back(NT - 1)


def kernel(x, adj, L0_gnn_weight, L0_gnn_bias):
    import numpy as np
    import concourse.bacc as bacc
    from concourse import mybir
    from concourse.bass_utils import run_bass_kernel_spmd

    tile, part = 512, 128
    n, c = x.shape
    nt, kb = n // tile, tile // part
    adj = np.asarray(adj)
    x = np.ascontiguousarray(x)
    adj_t = np.ascontiguousarray(
        adj.reshape(nt, tile, nt, kb, part).transpose(0, 2, 4, 3, 1)).reshape(nt, nt, part, kb * tile)
    arrays = {
        "adj_t": adj_t, "x": x, "x_t": np.ascontiguousarray(x.T),
        "weight": np.ascontiguousarray(L0_gnn_weight), "bias": np.ascontiguousarray(L0_gnn_bias),
    }
    nc = bacc.Bacc("TRN2", target_bir_lowering=False, num_devices=1)
    aps = {name: nc.dram_tensor(name, a.shape, mybir.dt.from_np(a.dtype), kind="ExternalInput").ap()
           for name, a in arrays.items()}
    aps["adj_t"] = aps["adj_t"].rearrange("i j p (k r) -> i j p k r", k=kb)
    out = nc.dram_tensor("out", (n, c), mybir.dt.float32, kind="ExternalOutput").ap()
    normalized_adjacency_layernorm(nc, aps["adj_t"], aps["x"], aps["x_t"], aps["weight"], aps["bias"], out)
    result = run_bass_kernel_spmd(nc, [arrays], core_ids=[0])
    return result.results[0]["out"]
```

```python
import concourse.bass as bass
from concourse import mybir
from contextlib import ExitStack


def normalized_adjacency_layernorm(nc, adj_t, x, x_t, weight, bias, parked, out):
    f32 = mybir.dt.float32
    f32r = mybir.dt.float32r
    ALU = mybir.AluOpType
    ACT = mybir.ActivationFunctionType

    P = 128
    N, C = x.shape
    TILE = adj_t.shape[-1]
    KB = TILE // P
    NT = N // TILE
    CELLS = KB * TILE
    EPS = 1e-5
    F32_MAX = 3.4028234e38

    BAND = 3
    RING = 6
    LEAD = 4
    PIECES = 2
    PK = KB // PIECES
    IN_FLIGHT = 3
    BANKS = 5
    PARKED = NT - 1 - BAND
    FIRST_DONE = NT - 1 - BAND
    TURNS = NT + PARKED

    def waiting_columns(row):
        return list(range(min(row + BAND, NT - 1), row - 1, -1))

    def load_order(row):
        lead = min(LEAD, row)
        only_summed = list(range(NT - 1, row + BAND, -1))
        waiting = waiting_columns(row)
        at_once = list(range(row - 1, -1, -1))
        return only_summed + at_once[:lead] + waiting + at_once[lead:]

    def at_once(row):
        return list(range(row - 1, -1, -1))

    def waited_for(col):
        return list(range(max(0, col - BAND), col + 1))

    def held_back(row):
        return 0 if row < 6 else 1 if row < 12 else 2

    def row_of(turn):
        return turn if turn < NT else NT + PARKED - 1 - turn

    def second_columns(turn):
        return list(range(row_of(turn) + BAND + 1, NT))

    def is_split(turn, col):
        return turn >= NT or (col == NT - 1 and turn >= FIRST_DONE)

    products = []
    for i in range(NT):
        products += [(i, j) for j in at_once(i)]
        products += [(k, i) for k in waited_for(i)]
    for t in range(NT, TURNS):
        products += [(t, j) for j in second_columns(t)]
    plain_no = {p: n for n, p in enumerate([p for p in products if not is_split(*p)])}
    split_products = [p for p in products if is_split(*p)]
    split_no = {p: n for n, p in enumerate(split_products)}
    first_of = {t: [p for p in products if p[0] == t][0] for t in range(TURNS)}
    last_of = {t: [p for p in products if p[0] == t][-1] for t in range(TURNS)}

    band_slot = [RING + d * (d + 1) // 2 for d in range(BAND + 1)]
    SLOTS = RING + (BAND + 1) * (BAND + 2) // 2
    FACTORS = NT - 1 - BAND
    FACTORS_IN_SLOT = CELLS // (2 * KB * C)

    ADDS = NT - 1 + 2

    def adds_through(row, position):
        return row * ADDS + max(position, 1)

    loads, slot_of, load_count = [], {}, {}
    uses, free_after, last_in_slot = [0] * SLOTS, [(0, 0, 0)] * SLOTS, [None] * SLOTS

    def load(turn, col, slot, adds):
        uses[slot] += 1
        loads.append((turn, col, slot, free_after[slot]))
        slot_of[turn, col], load_count[turn, col] = slot, uses[slot]
        free_after[slot] = (adds, plain_no.get((turn, col), -1) + 1, PIECES * (split_no.get((turn, col), -1) + 1))
        if turn < NT:
            last_in_slot[slot] = (turn, col)

    second_pass = [(t, j) for t in range(NT, TURNS) for j in second_columns(t)]
    second_slots = []
    passing = 0
    for t in range(NT):
        for pos, j in enumerate(load_order(t)):
            if 0 <= j - t <= BAND:
                load(t, j, band_slot[j - t] + t % (j - t + 1), adds_through(t, pos))
            else:
                load(t, j, passing % RING, adds_through(t, pos))
                passing += 1
            if j == t:
                for dist in range(NT - t, BAND + 1):
                    second_slots.append(band_slot[dist] + (t - 1 - dist) % (dist + 1))
                    load(*second_pass[len(second_slots) - 1], second_slots[-1], 0)
    second_slots += [slot_of[k, NT - 1] for k in waited_for(NT - 1)]
    for n in range(BAND * (BAND + 1) // 2, len(second_pass)):
        load(*second_pass[n], second_slots[n % len(second_slots)], 0)

    WHOLE, TURN_BACK, RESIDUAL, SQUARES, VARIANCE, SHIFT, STORE = 1, 2, 3, 4, 5, 6, 7
    APART = 3
    last_steps_from = []
    for e in range(NT):
        done = split_no[last_of[FIRST_DONE + e]]
        last_steps_from.append(max(done, last_steps_from[-1] + APART) if e else done)

    def now(step, n):
        return [e for e in range(NT) if last_steps_from[e] + step == n]

    ROUNDS = last_steps_from[-1] + STORE + 1

    with ExitStack() as ctx:
        def sb(name, shape, dt=f32):
            return ctx.enter_context(nc.sbuf_tensor(name, shape, dt))

        def ps(name, shape):
            return ctx.enter_context(nc.psum_tensor(name, shape, f32))

        def sem(name):
            return ctx.enter_context(nc.semaphore(name))

        scaled = sb("scaled", [P, NT * KB, C])
        sums = sb("sums", [P, 2, CELLS])
        tiles_waiting = sb("tiles_waiting", [P, SLOTS - RING, CELLS])
        tile_hi = sb("tile_hi", [P, IN_FLIGHT, PK * TILE], f32r)
        tile_lo = sb("tile_lo", [P, IN_FLIGHT, PK * TILE], f32r)
        park_out = sb("park_out", [P, TILE])
        xt_in = sb("xt_in", [P, TILE])
        w_in = sb("w_in", [P, C])
        ident = sb("ident", [P, P])
        bias_in = sb("bias_in", [P, C])
        ones = sb("ones", [P, 1])
        minus_half = sb("minus_half", [P, KB])
        zeros = sb("zeros", [P, KB])
        degree = sb("degree", [P, NT, KB])
        d = sb("d", [P, NT, KB])
        is_inf = sb("is_inf", [P, KB], mybir.dt.int32)
        z_sum = sb("z_sum", [P, 2, KB])
        minus_mean = sb("minus_mean", [P, 2, KB])
        square_sum = sb("square_sum", [P, 2, KB])
        variance = sb("variance", [P, 2, KB])
        rstd = sb("rstd", [P, 2, KB])
        shift = sb("shift", [P, 2, KB])
        whole_t = sums[:, 0, 0:2 * TILE].rearrange("p (b i) -> p b i", b=2)
        z = sums[:, 0, 2 * TILE:4 * TILE].rearrange("p (b i c) -> p b i c", b=2, c=C)
        x_in = sums[:, 1, 0:2 * TILE].rearrange("p (b i c) -> p b i c", b=2, c=C)
        squares = sums[:, 1, 2 * TILE:3 * TILE].rearrange("p (i c) -> p i c", c=C)
        park_in = sums[:, 1, 3 * TILE:4 * TILE]
        with nc.sbuf_tensor("tiles_passing", [P, RING, CELLS], f32) as tiles_passing:
            pass
        factors = sb("factors", [P, FACTORS, 2, KB, C], f32r)

        def in_slot(slot):
            return tiles_passing[:, slot, :] if slot < RING else tiles_waiting[:, slot - RING, :]

        def tile(t, j):
            return in_slot(slot_of[t, j])

        def factor_no(j):
            return NT - 1 - j

        acc = [ps(f"acc{b}", [P, TILE]) for b in range(BANKS)]
        degree_ps = ps("degree_ps", [P, 2, KB])
        turned = [ps(f"turned{b}", [P, KB, C]) for b in range(2)]

        tile_loaded = [sem(f"tile_loaded{s}") for s in range(SLOTS)]
        xt_loaded = sem("xt_loaded")
        x_loaded = [sem(f"x_loaded{b}") for b in range(2)]
        y_stored = [sem(f"y_stored{b}") for b in range(2)]
        park_stored = sem("park_stored")
        park_loaded = sem("park_loaded")
        consts_loaded = sem("consts_loaded")
        consts_set = sem("consts_set")
        ident_cleared = sem("ident_cleared")
        ident_ready = sem("ident_ready")
        added = sem("added")
        multiplied = sem("multiplied")
        piece_multiplied = sem("piece_multiplied")
        hi_ready = sem("hi_ready")
        lo_ready = sem("lo_ready")
        factor_hi_ready = sem("factor_hi_ready")
        factor_lo_ready = sem("factor_lo_ready")
        xw_product = sem("xw_product")
        xw_saved = sem("xw_saved")
        degree_product = sem("degree_product")
        degree_saved = sem("degree_saved")
        powered = sem("powered")
        masked = sem("masked")
        d_ready = sem("d_ready")
        scaled_ready = sem("scaled_ready")
        park_ready = sem("park_ready")
        whole_ready = sem("whole_ready")
        turned_back = sem("turned_back")
        xb_ready = sem("xb_ready")
        z_ready = sem("z_ready")
        mean_ready = sem("mean_ready")
        squared = sem("squared")
        variance_ready = sem("variance_ready")
        rstd_ready = sem("rstd_ready")
        shift_ready = sem("shift_ready")
        y_ready = sem("y_ready")

        rows_of = x.rearrange("(t k p) c -> t p k c", k=KB, p=P)
        out_rows = out.rearrange("(t k p) c -> t p k c", k=KB, p=P)

        def wait_loaded(eng, t, j):
            eng.wait_ge(tile_loaded[slot_of[t, j]], 16 * load_count[t, j])

        def wait_product(eng, t, j):
            if is_split(t, j):
                eng.wait_ge(piece_multiplied, PIECES * (split_no[t, j] + 1))
            else:
                eng.wait_ge(multiplied, plain_no[t, j] + 1)

        def wait_factor_memory(eng, j):
            wait_product(eng, *last_in_slot[factor_no(j) // FACTORS_IN_SLOT])

        def brings_factor(t, j):
            return (t, j) == (FIRST_DONE, NT - 1) or (t > NT and (t, j) == first_of[t])

        block = ctx.enter_context(nc.Block())

        @block.sync
        def _(sp):
            sp.dma_start(w_in[:, :], weight[:, :]).then_inc(consts_loaded, 16)
            sp.dma_start(bias_in[:, :], bias.rearrange("(a c) -> a c", a=1).to_broadcast([P, C])
                         ).then_inc(consts_loaded, 16)
            for n, (t, j, slot, (adds, plain, pieces)) in enumerate(loads):
                if t < NT and j == load_order(t)[0]:
                    if t >= 1:
                        sp.wait_ge(xw_product, t)
                    sp.dma_start(xt_in[:, :], x_t[:, t * TILE:(t + 1) * TILE]).then_inc(xt_loaded, 16)
                if adds:
                    sp.wait_ge(added, adds)
                if plain:
                    sp.wait_ge(multiplied, plain)
                if pieces:
                    sp.wait_ge(lo_ready, pieces)
                sp.dma_start(in_slot(slot), adj_t[row_of(t), j]).then_inc(tile_loaded[slot], 16)

        @block.vector
        def _(dve):
            nc.vector.memset(ones[:, :], 1.0)
            nc.vector.memset(minus_half[:, :], -0.5)
            nc.vector.memset(zeros[:, :], 0.0).then_inc(consts_set, 1)

            def degree_guard(i):
                dve.wait_ge(powered, i + 1)
                nc.vector.tensor_scalar(is_inf[:, :], d[:, i, :], F32_MAX, None, ALU.is_gt
                                        ).then_inc(masked, 1)
                dve.wait_ge(masked, i + 1)
                nc.vector.copy_predicated(d[:, i, :], is_inf[:, :], zeros[:, :]).then_inc(d_ready, 1)

            def rest_of_factor(j):
                dve.wait_ge(factor_hi_ready, factor_no(j) + 1)
                wait_factor_memory(dve, j)
                nc.vector.tensor_tensor(factors[:, factor_no(j), 1], scaled[:, j * KB:(j + 1) * KB, :],
                                        factors[:, factor_no(j), 0].bitcast(f32), ALU.subtract
                                        ).then_inc(factor_lo_ready, 1)

            def rest_of_piece(t, j, q):
                m = PIECES * split_no[t, j] + q
                dve.wait_ge(hi_ready, m + 1)
                wait_loaded(dve, t, j)
                if m >= IN_FLIGHT:
                    dve.wait_ge(piece_multiplied, m - IN_FLIGHT + 1)
                span = slice(q * PK * TILE, (q + 1) * PK * TILE)
                nc.vector.tensor_tensor(tile_lo[:, m % IN_FLIGHT, :], tile(t, j)[:, span],
                                        tile_hi[:, m % IN_FLIGHT, :].bitcast(f32), ALU.subtract
                                        ).then_inc(lo_ready, 1)

            for i in range(NT):
                order = load_order(i)
                for pos in range(1, NT):
                    for j in (order[0:2] if pos == 1 else order[pos:pos + 1]):
                        wait_loaded(dve, i, j)
                    total = sums[:, i % 2, :]
                    before = tile(i, order[0])
                    if pos == 1:
                        if i >= 2:
                            dve.wait_ge(degree_product, i - 1)
                    else:
                        before = total
                        dve.wait_ge(added, adds_through(i, pos) - 1)
                    nc.vector.tensor_tensor(total, before, tile(i, order[pos]), ALU.add).then_inc(added, 1)
                    if pos == 1 and i >= 1:
                        degree_guard(i - 1)
                for half in (2 * TILE, TILE):
                    dve.wait_ge(added, (i + 1) * ADDS - (2 if half == 2 * TILE else 1))
                    nc.vector.tensor_tensor(total[:, 0:half], total[:, 0:half], total[:, half:2 * half],
                                            ALU.add).then_inc(added, 1)
            degree_guard(NT - 1)

            def whole(e):
                t = FIRST_DONE + e
                wait_product(dve, *last_of[t])
                if e >= 2:
                    dve.wait_ge(turned_back, e - 1)
                if t < NT:
                    nc.vector.tensor_copy(whole_t[:, e % 2, :], acc[t % BANKS][:, :]
                                          ).then_inc(whole_ready, 1)
                else:
                    dve.wait_ge(park_loaded, 16 * (t - NT + 1))
                    nc.vector.tensor_tensor(whole_t[:, e % 2, :], acc[t % BANKS][:, :], park_in, ALU.add
                                            ).then_inc(whole_ready, 1)

            def residual(e):
                b, r = e % 2, row_of(FIRST_DONE + e)
                dve.wait_ge(xb_ready, e + 1)
                dve.wait_ge(turned_back, e + 1)
                if e >= 2:
                    dve.wait_ge(y_stored[b], 16 * (e // 2))
                for k in range(KB):
                    nc.vector.scalar_tensor_tensor(z[:, b, k, :], turned[b][:, k, :], d[:, r, k:k + 1],
                                                   x_in[:, b, k, :], ALU.mult, ALU.add,
                                                   accum_out=z_sum[:, b, k:k + 1]).then_inc(z_ready, 1)
                dve.wait_ge(z_ready, KB * (e + 1))
                nc.vector.tensor_scalar(minus_mean[:, b, :], z_sum[:, b, :], -1.0 / C, None, ALU.mult
                                        ).then_inc(mean_ready, 1)

            def deviation(e):
                b = e % 2
                dve.wait_ge(squared, KB * (e + 1))
                nc.vector.tensor_scalar(variance[:, b, :], square_sum[:, b, :], 1.0 / C, EPS,
                                        ALU.mult, ALU.add).then_inc(variance_ready, 1)

            def mean_shift(e):
                b = e % 2
                dve.wait_ge(rstd_ready, e + 1)
                nc.vector.tensor_tensor(shift[:, b, :], minus_mean[:, b, :], rstd[:, b, :], ALU.mult
                                        ).then_inc(shift_ready, 1)

            for n in range(split_no[FIRST_DONE, NT - 1], ROUNDS):
                if n < len(split_products):
                    t, j = split_products[n]
                    if brings_factor(t, j):
                        rest_of_factor(j)
                    for q in range(PIECES):
                        rest_of_piece(t, j, q)
                for step, do in ((WHOLE, whole), (RESIDUAL, residual), (VARIANCE, deviation),
                                 (SHIFT, mean_shift)):
                    for e in now(step, n):
                        do(e)

        @block.gpsimd
        def _(pool):
            nc.gpsimd.memset(ident[:, :], 0.0).then_inc(ident_cleared, 1)
            pool.wait_ge(ident_cleared, 1)
            nc.gpsimd.affine_select(out=ident[:, :], in_=ident[:, :], compare_op=ALU.not_equal, fill=1.0,
                                    base=0, pattern=[[-1, P]], channel_multiplier=1).then_inc(ident_ready, 1)
            pool.wait_ge(consts_set, 1)
            for i in range(NT):
                pool.wait_ge(degree_saved, i + 1)
                nc.gpsimd.tensor_tensor(d[:, i, :], degree[:, i, :], minus_half[:, :], ALU.pow
                                        ).then_inc(powered, 1)
            pool.wait_ge(consts_loaded, 32)
            for e in range(NT):
                pool.wait_ge(x_loaded[e % 2], 16 * (e // 2 + 1))
                nc.gpsimd.tensor_tensor(x_in[:, e % 2], x_in[:, e % 2],
                                        bias_in[:, None, :].to_broadcast([P, KB, C]), ALU.add
                                        ).then_inc(xb_ready, 1)
                pool.wait_ge(variance_ready, e + 1)
                nc.gpsimd.tensor_tensor(rstd[:, e % 2, :], variance[:, e % 2, :], minus_half[:, :], ALU.pow
                                        ).then_inc(rstd_ready, 1)

        @block.scalar
        def _(act):
            def round_factor(j):
                wait_factor_memory(act, j)
                act.wait_ge(scaled_ready, KB * (j + 1))
                nc.scalar.activation(factors[:, factor_no(j), 0], scaled[:, j * KB:(j + 1) * KB, :], ACT.Copy
                                     ).then_inc(factor_hi_ready, 1)

            def round_piece(t, j, q):
                m = PIECES * split_no[t, j] + q
                wait_loaded(act, t, j)
                if m >= IN_FLIGHT:
                    act.wait_ge(piece_multiplied, m - IN_FLIGHT + 1)
                span = slice(q * PK * TILE, (q + 1) * PK * TILE)
                nc.scalar.activation(tile_hi[:, m % IN_FLIGHT, :], tile(t, j)[:, span], ACT.Copy
                                     ).then_inc(hi_ready, 1)

            def load_rows(e):
                act.dma_start(x_in[:, e % 2], rows_of[row_of(FIRST_DONE + e)]).then_inc(x_loaded[e % 2], 16)

            for i in range(NT):
                act.wait_ge(xw_product, i + 1)
                nc.scalar.activation(scaled[:, i * KB:(i + 1) * KB, :], turned[i % 2][:, :, :], ACT.Copy
                                     ).then_inc(xw_saved, 1)
                act.wait_ge(degree_product, i + 1)
                nc.scalar.activation(degree[:, i, :], degree_ps[:, i % 2, :], ACT.Copy).then_inc(degree_saved, 1)
                act.wait_ge(d_ready, i + 1)
                act.wait_ge(xw_saved, i + 1)
                for k in range(KB):
                    nc.scalar.activation(scaled[:, i * KB + k, :], scaled[:, i * KB + k, :], ACT.Copy,
                                         scale=d[:, i, k:k + 1]).then_inc(scaled_ready, 1)
                if BAND <= i < NT - 1:
                    wait_product(act, i - BAND, i)
                    if i > BAND:
                        act.wait_ge(park_stored, 16 * (i - BAND))
                    nc.scalar.activation(park_out[:, :], acc[(i - BAND) % BANKS][:, :], ACT.Copy
                                         ).then_inc(park_ready, 1)
                    act.wait_ge(park_ready, i - BAND + 1)
                    act.dma_start(parked[i - BAND], park_out[:, :]).then_inc(park_stored, 16)
            act.wait_ge(degree_product, NT)
            load_rows(0)
            load_rows(1)

            def load_parked(t):
                if t == NT:
                    act.wait_ge(park_stored, 16 * PARKED)
                else:
                    act.wait_ge(whole_ready, BAND + 1 + t - NT)
                act.dma_start(park_in, parked[row_of(t)]).then_inc(park_loaded, 16)

            def squares_of(e):
                b = e % 2
                act.wait_ge(mean_ready, e + 1)
                for k in range(KB):
                    nc.scalar.activation(squares[:, k, :], z[:, b, k, :], ACT.Square,
                                         bias=minus_mean[:, b, k:k + 1],
                                         accum_out=square_sum[:, b, k:k + 1]).then_inc(squared, 1)
                if e + 2 < NT:
                    load_rows(e + 2)

            def store(e):
                b = e % 2
                act.wait_ge(squared, KB * (e + 1))
                act.wait_ge(shift_ready, e + 1)
                for k in range(KB):
                    nc.scalar.activation(z[:, b, k, :], z[:, b, k, :], ACT.Identity,
                                         bias=shift[:, b, k:k + 1], scale=rstd[:, b, k:k + 1]
                                         ).then_inc(y_ready, 1)
                act.wait_ge(y_ready, KB * (e + 1))
                act.dma_start(out_rows[row_of(FIRST_DONE + e)], z[:, b]).then_inc(y_stored[b], 16)

            load_parked(NT)
            for n in range(split_no[FIRST_DONE, NT - 1], ROUNDS):
                if n < len(split_products):
                    t, j = split_products[n]
                    if brings_factor(t, j):
                        round_factor(j)
                    for q in range(PIECES):
                        round_piece(t, j, q)
                for e in now(SQUARES, n):
                    squares_of(e)
                for e in now(STORE, n):
                    store(e)
                for e in now(WHOLE + 1, n):
                    if BAND < e < NT - 1:
                        load_parked(FIRST_DONE + e + 1)
            for b in range(2):
                act.wait_ge(y_stored[b], 16 * (NT // 2))

        @block.tensor
        def _(pe):
            def xw(i):
                pe.wait_ge(xt_loaded, 16 * (i + 1))
                if i == 0:
                    pe.wait_ge(consts_loaded, 32)
                if i >= 2:
                    pe.wait_ge(xw_saved, i - 1)
                for k in range(KB):
                    last = nc.tensor.matmul(turned[i % 2][:, k, :], xt_in[:, k * P:(k + 1) * P],
                                            w_in[:, :], start=True, stop=True)
                last.then_inc(xw_product, 1)

            def degrees(i):
                pe.wait_ge(added, (i + 1) * ADDS)
                if i == 0:
                    pe.wait_ge(consts_set, 1)
                if i >= 2:
                    pe.wait_ge(degree_saved, i - 1)
                for m in range(KB):
                    last = nc.tensor.matmul(degree_ps[:, i % 2, m:m + 1], sums[:, i % 2, m * P:(m + 1) * P],
                                            ones[:, :], start=True, stop=True)
                last.then_inc(degree_product, 1)

            def multiply(t, j):
                first, last = (t, j) == first_of[t], (t, j) == last_of[t]
                if first and t >= BANKS:
                    before = t - BANKS
                    if before < FIRST_DONE:
                        pe.wait_ge(park_ready, before + 1)
                    else:
                        pe.wait_ge(whole_ready, before - FIRST_DONE + 1)
                if is_split(t, j):
                    multiply_split(t, j, first, last)
                    return
                wait_loaded(pe, t, j)
                pe.wait_ge(scaled_ready, KB * (j + 1))
                for k in range(KB):
                    mm = nc.tensor.matmul(acc[t % BANKS][:, :], scaled[:, j * KB + k, :],
                                          tile(t, j)[:, k * TILE:(k + 1) * TILE],
                                          start=(first and k == 0), stop=(last and k == KB - 1))
                mm.then_inc(multiplied, 1)

            def multiply_split(t, j, first, last):
                pe.wait_ge(factor_lo_ready, factor_no(j) + 1)
                bank = acc[t % BANKS][:, :]
                for q in range(PIECES):
                    m = PIECES * split_no[t, j] + q
                    pe.wait_ge(hi_ready, m + 1)
                    for k in range(PK):
                        hi, lo = (factors[:, factor_no(j), part, q * PK + k, :] for part in (0, 1))
                        moving = tile_hi[:, m % IN_FLIGHT, k * TILE:(k + 1) * TILE]
                        nc.tensor.matmul(bank, lo, moving, start=(first and q == 0 and k == 0), stop=False)
                        nc.tensor.matmul(bank, hi, moving, start=False, stop=False)
                    pe.wait_ge(lo_ready, m + 1)
                    for k in range(PK):
                        mm = nc.tensor.matmul(bank, factors[:, factor_no(j), 0, q * PK + k, :],
                                              tile_lo[:, m % IN_FLIGHT, k * TILE:(k + 1) * TILE],
                                              start=False, stop=(last and q == PIECES - 1 and k == PK - 1))
                    mm.then_inc(piece_multiplied, 1)

            def turn_back(e):
                pe.wait_ge(whole_ready, e + 1)
                if e >= 2:
                    pe.wait_ge(z_ready, KB * (e - 1))
                else:
                    pe.wait_ge(xw_saved, NT)
                if e == 0:
                    pe.wait_ge(ident_ready, 1)
                for k in range(KB):
                    last = nc.tensor.transpose(turned[e % 2][:, k, :], whole_t[:, e % 2, k * P:(k + 1) * P],
                                               ident[:, :])
                last.then_inc(turned_back, 1)

            for i in range(NT):
                xw(i)
                early = len(at_once(i)) - held_back(i)
                for j in at_once(i)[:early]:
                    multiply(i, j)
                degrees(i)
                for j in at_once(i)[early:]:
                    multiply(i, j)
                if i < NT - 1:
                    for k in waited_for(i):
                        multiply(k, i)
            for n in range(split_no[FIRST_DONE, NT - 1], ROUNDS):
                if n < len(split_products):
                    multiply(*split_products[n])
                for e in now(TURN_BACK, n):
                    turn_back(e)


def kernel(x, adj, L0_gnn_weight, L0_gnn_bias):
    import numpy as np
    import concourse.bacc as bacc
    from concourse import mybir
    from concourse.bass_utils import run_bass_kernel_spmd

    tile, part = 512, 128
    n, c = x.shape
    nt, kb = n // tile, tile // part
    adj = np.asarray(adj)
    x = np.ascontiguousarray(x)
    adj_t = np.ascontiguousarray(
        adj.reshape(nt, tile, nt, kb, part).transpose(0, 2, 4, 3, 1)).reshape(nt, nt, part, kb * tile)
    arrays = {
        "adj_t": adj_t, "x": x, "x_t": np.ascontiguousarray(x.T),
        "weight": np.ascontiguousarray(L0_gnn_weight), "bias": np.ascontiguousarray(L0_gnn_bias),
    }
    nc = bacc.Bacc("TRN2", target_bir_lowering=False, num_devices=1)
    aps = {name: nc.dram_tensor(name, a.shape, mybir.dt.from_np(a.dtype), kind="ExternalInput").ap()
           for name, a in arrays.items()}
    aps["adj_t"] = aps["adj_t"].rearrange("i j p (k r) -> i j p k r", k=kb)
    parked = nc.dram_tensor("parked", (nt, part, tile), mybir.dt.float32, kind="Internal").ap()
    out = nc.dram_tensor("out", (n, c), mybir.dt.float32, kind="ExternalOutput").ap()
    normalized_adjacency_layernorm(nc, aps["adj_t"], aps["x"], aps["x_t"], aps["weight"], aps["bias"], parked, out)
    result = run_bass_kernel_spmd(nc, [arrays], core_ids=[0])
    return result.results[0]["out"]
```

```python
import concourse.bass as bass
from concourse import mybir
from contextlib import ExitStack


def normalized_adjacency_layernorm(nc, adj_t, x, x_t, weight, bias, parked, out):
    f32 = mybir.dt.float32
    f32r = mybir.dt.float32r
    ALU = mybir.AluOpType
    ACT = mybir.ActivationFunctionType

    P = 128
    N, C = x.shape
    TILE = adj_t.shape[-1]
    KB = TILE // P
    NT = N // TILE
    CELLS = KB * TILE
    EPS = 1e-5
    F32_MAX = 3.4028234e38

    BAND = 3
    RING = 6
    LEAD = 6
    PIECES = 2
    PK = KB // PIECES
    IN_FLIGHT = 3
    BANKS = 6

    SCALED_IN_SLOT = CELLS // (KB * C)
    PIECE_SLOTS = 2 * IN_FLIGHT // PIECES
    OWN, LENT_BY_SCALED = "own", "scaled"
    PLACES = [(0, NT - 1), (OWN, NT), (1, NT - 1), (2, NT - 1), (LENT_BY_SCALED, NT - SCALED_IN_SLOT)]
    assert len(PLACES) == BAND + 2 and PIECE_SLOTS == 3

    def finds_a_place(row, col):
        return col - row == BAND + 1 and col < PLACES[row % (BAND + 2)][1]

    def waiting_columns(row):
        return [j for j in range(NT - 1, row - 1, -1) if j - row <= BAND or finds_a_place(row, j)]

    def load_order(row):
        lead = min(LEAD, row)
        only_summed = [j for j in range(NT - 1, row, -1) if j not in waiting_columns(row)]
        waiting = waiting_columns(row)
        return only_summed + at_once(row)[:lead] + waiting + at_once(row)[lead:]

    def at_once(row):
        return list(range(row - 1, -1, -1))

    def waited_for(col):
        return [i for i in range(col + 1) if col in waiting_columns(i)]

    def held_back(row):
        return 0 if row < 6 else 1 if row < 12 else 2

    FIRST_DONE = min(i for i in range(NT) if len(waiting_columns(i)) == NT - i)
    PARKED = FIRST_DONE
    TURNS = NT + PARKED

    def row_of(turn):
        return turn if turn < NT else NT + PARKED - 1 - turn

    def second_columns(turn):
        row = row_of(turn)
        return [j for j in range(row, NT) if j not in waiting_columns(row)]

    def is_split(turn, col):
        return turn >= NT or (col == NT - 1 and turn >= FIRST_DONE)

    products = []
    for i in range(NT):
        products += [(i, j) for j in at_once(i)]
        products += [(k, i) for k in waited_for(i)]
    for t in range(NT, TURNS):
        products += [(t, j) for j in second_columns(t)]
    plain_no = {p: n for n, p in enumerate([p for p in products if not is_split(*p)])}
    split_products = [p for p in products if is_split(*p)]
    split_no = {p: n for n, p in enumerate(split_products)}
    first_of = {t: [p for p in products if p[0] == t][0] for t in range(TURNS)}
    last_of = {t: [p for p in products if p[0] == t][-1] for t in range(TURNS)}

    band_slot = [RING + d * (d + 1) // 2 for d in range(BAND + 1)]
    FIRST_PLACE = RING + (BAND + 1) * (BAND + 2) // 2
    SLOTS = FIRST_PLACE + len(PLACES)
    factor_no = {j: n for n, j in enumerate(dict.fromkeys(j for _, j in split_products))}
    takes_first = {j: [p for p in split_products if p[1] == j][0] for j in factor_no}
    FACTORS = len(factor_no)
    FACTORS_IN_SLOT = CELLS // (2 * KB * C)

    ADDS = NT - 1 + 2

    def adds_through(row, position):
        return row * ADDS + max(position, 1)

    loads, slot_of, load_count = [], {}, {}
    uses, free_after, last_in_slot = [0] * SLOTS, [(0, 0, 0)] * SLOTS, [None] * SLOTS

    def load(turn, col, slot, adds):
        uses[slot] += 1
        loads.append((turn, col, slot, free_after[slot]))
        slot_of[turn, col], load_count[turn, col] = slot, uses[slot]
        free_after[slot] = (adds, plain_no.get((turn, col), -1) + 1, PIECES * (split_no.get((turn, col), -1) + 1))
        if turn < NT:
            last_in_slot[slot] = (turn, col)

    second_pass = [(t, j) for t in range(NT, TURNS) for j in second_columns(t)]
    second_slots = []
    passing = 0
    for t in range(NT):
        for pos, j in enumerate(load_order(t)):
            if finds_a_place(t, j):
                load(t, j, FIRST_PLACE + t % (BAND + 2), adds_through(t, pos))
            elif 0 <= j - t <= BAND:
                load(t, j, band_slot[j - t] + t % (j - t + 1), adds_through(t, pos))
            else:
                load(t, j, passing % RING, adds_through(t, pos))
                passing += 1
            if j == t:
                for dist in range(NT - t, BAND + 1):
                    second_slots.append(band_slot[dist] + (t - 1 - dist) % (dist + 1))
                    load(*second_pass[len(second_slots) - 1], second_slots[-1], 0)
    loaded_early = len(second_slots)
    second_slots += [slot_of[k, NT - 1] for k in waited_for(NT - 1)]
    for n in range(loaded_early, len(second_pass)):
        load(*second_pass[n], second_slots[n % len(second_slots)], 0)

    WHOLE, TURN_BACK, RESIDUAL, SQUARES, VARIANCE, SHIFT, STORE = 1, 2, 3, 4, 5, 6, 7
    APART = 4
    last_steps_from = []
    for e in range(NT):
        done = split_no[last_of[FIRST_DONE + e]]
        last_steps_from.append(max(done, last_steps_from[-1] + APART) if e else done)

    def now(step, n):
        return [e for e in range(NT) if last_steps_from[e] + step == n]

    ROUNDS = last_steps_from[-1] + STORE + 1

    with ExitStack() as ctx:
        def sb(name, shape, dt=f32):
            return ctx.enter_context(nc.sbuf_tensor(name, shape, dt))

        def ps(name, shape):
            return ctx.enter_context(nc.psum_tensor(name, shape, f32))

        def sem(name):
            return ctx.enter_context(nc.semaphore(name))

        with nc.sbuf_tensor("scaled_as_tiles", [P, NT // SCALED_IN_SLOT, CELLS], f32) as scaled_as_tiles:
            pass
        scaled = sb("scaled", [P, NT * KB, C])
        sums = sb("sums", [P, CELLS])
        folded = sb("folded", [P, TILE])
        tiles_waiting = sb("tiles_waiting", [P, FIRST_PLACE - RING + 1, CELLS])
        with nc.sbuf_tensor("pieces_as_tiles", [P, PIECE_SLOTS, CELLS], f32) as pieces_as_tiles:
            pass
        tile_hi = sb("tile_hi", [P, IN_FLIGHT, PK * TILE], f32r)
        tile_lo = sb("tile_lo", [P, IN_FLIGHT, PK * TILE], f32r)
        park_out = sb("park_out", [P, TILE])
        xt_in = sb("xt_in", [P, TILE])
        w_in = sb("w_in", [P, C])
        ident = sb("ident", [P, P])
        ones = sb("ones", [P, 1])
        minus_half = sb("minus_half", [P, KB])
        zeros = sb("zeros", [P, KB])
        degree = sb("degree", [P, NT, KB])
        d = sb("d", [P, NT, KB])
        is_inf = sb("is_inf", [P, KB], mybir.dt.int32)
        z_sum = sb("z_sum", [P, 2, KB])
        minus_mean = sb("minus_mean", [P, 2, KB])
        square_sum = sb("square_sum", [P, 2, KB])
        variance = sb("variance", [P, 2, KB])
        rstd = sb("rstd", [P, 2, KB])
        shift = sb("shift", [P, 2, KB])
        z = sums[:, 0:2 * TILE].rearrange("p (b i c) -> p b i c", b=2, c=C)
        x_in = sums[:, 2 * TILE:4 * TILE].rearrange("p (b i c) -> p b i c", b=2, c=C)
        squares = folded.rearrange("p (i c) -> p i c", c=C)
        park_in = xt_in
        bias_in = w_in
        with nc.sbuf_tensor("tiles_passing", [P, RING, CELLS], f32) as tiles_passing:
            pass
        factors = sb("factors", [P, FACTORS, 2, KB, C], f32r)
        whole_t = sb("whole_t", [P, 2, TILE])

        def in_slot(slot):
            if slot < RING:
                return tiles_passing[:, slot, :]
            if slot < FIRST_PLACE:
                return tiles_waiting[:, slot - RING, :]
            place = PLACES[slot - FIRST_PLACE][0]
            if place == OWN:
                return tiles_waiting[:, FIRST_PLACE - RING, :]
            if place == LENT_BY_SCALED:
                return scaled_as_tiles[:, NT // SCALED_IN_SLOT - 1, :]
            return pieces_as_tiles[:, place, :]

        def tile(t, j):
            return in_slot(slot_of[t, j])

        acc = [ps(f"acc{b}", [P, TILE]) for b in range(BANKS)]
        turned = [ps(f"turned{b}", [P, KB, C]) for b in range(2)]
        xw_ps = turned[0]
        degree_ps = turned[1][:, 0, 0:2 * KB].rearrange("p (b k) -> p b k", b=2)

        tile_loaded = [sem(f"tile_loaded{s}") for s in range(SLOTS)]
        xt_loaded = sem("xt_loaded")
        x_loaded = [sem(f"x_loaded{b}") for b in range(2)]
        y_stored = [sem(f"y_stored{b}") for b in range(2)]
        park_stored = sem("park_stored")
        park_loaded = sem("park_loaded")
        weight_loaded = sem("weight_loaded")
        bias_loaded = sem("bias_loaded")
        consts_set = sem("consts_set")
        ident_cleared = sem("ident_cleared")
        ident_ready = sem("ident_ready")
        added = sem("added")
        multiplied = sem("multiplied")
        piece_multiplied = sem("piece_multiplied")
        hi_ready = sem("hi_ready")
        lo_ready = sem("lo_ready")
        factor_hi_ready = sem("factor_hi_ready")
        factor_lo_ready = sem("factor_lo_ready")
        xw_product = sem("xw_product")
        xw_saved = sem("xw_saved")
        degree_product = sem("degree_product")
        degree_saved = sem("degree_saved")
        powered = sem("powered")
        masked = sem("masked")
        d_ready = sem("d_ready")
        scaled_ready = sem("scaled_ready")
        park_ready = sem("park_ready")
        whole_ready = sem("whole_ready")
        turned_back = sem("turned_back")
        xb_ready = sem("xb_ready")
        z_ready = sem("z_ready")
        mean_ready = sem("mean_ready")
        squared = sem("squared")
        variance_ready = sem("variance_ready")
        rstd_ready = sem("rstd_ready")
        shift_ready = sem("shift_ready")
        y_ready = sem("y_ready")

        rows_of = x.rearrange("(t k p) c -> t p k c", k=KB, p=P)
        out_rows = out.rearrange("(t k p) c -> t p k c", k=KB, p=P)

        def wait_loaded(eng, t, j):
            eng.wait_ge(tile_loaded[slot_of[t, j]], 16 * load_count[t, j])

        def wait_product(eng, t, j):
            if is_split(t, j):
                eng.wait_ge(piece_multiplied, PIECES * (split_no[t, j] + 1))
            else:
                eng.wait_ge(multiplied, plain_no[t, j] + 1)

        def wait_factor_memory(eng, j):
            wait_product(eng, *last_in_slot[factor_no[j] // FACTORS_IN_SLOT])

        def brings_factor(t, j):
            return (t, j) == takes_first[j]

        block = ctx.enter_context(nc.Block())

        @block.sync
        def _(sp):
            sp.dma_start(w_in[:, :], weight[:, :]).then_inc(weight_loaded, 16)
            for n, (t, j, slot, (adds, plain, pieces)) in enumerate(loads):
                if t < NT and j == load_order(t)[0]:
                    if t >= 1:
                        sp.wait_ge(xw_product, t)
                    sp.dma_start(xt_in[:, :], x_t[:, t * TILE:(t + 1) * TILE]).then_inc(xt_loaded, 16)
                if adds:
                    sp.wait_ge(added, adds)
                if plain:
                    sp.wait_ge(multiplied, plain)
                if pieces:
                    sp.wait_ge(lo_ready, pieces)
                sp.dma_start(in_slot(slot), adj_t[row_of(t), j]).then_inc(tile_loaded[slot], 16)

        @block.vector
        def _(dve):
            nc.vector.memset(ones[:, :], 1.0)
            nc.vector.memset(minus_half[:, :], -0.5)
            nc.vector.memset(zeros[:, :], 0.0).then_inc(consts_set, 1)

            def degree_guard(i):
                dve.wait_ge(powered, i + 1)
                nc.vector.tensor_scalar(is_inf[:, :], d[:, i, :], F32_MAX, None, ALU.is_gt
                                        ).then_inc(masked, 1)
                dve.wait_ge(masked, i + 1)
                nc.vector.copy_predicated(d[:, i, :], is_inf[:, :], zeros[:, :]).then_inc(d_ready, 1)

            def rest_of_factor(j):
                dve.wait_ge(factor_hi_ready, factor_no[j] + 1)
                wait_factor_memory(dve, j)
                nc.vector.tensor_tensor(factors[:, factor_no[j], 1], scaled[:, j * KB:(j + 1) * KB, :],
                                        factors[:, factor_no[j], 0].bitcast(f32), ALU.subtract
                                        ).then_inc(factor_lo_ready, 1)

            def rest_of_piece(t, j, q):
                m = PIECES * split_no[t, j] + q
                dve.wait_ge(hi_ready, m + 1)
                wait_loaded(dve, t, j)
                if m >= IN_FLIGHT:
                    dve.wait_ge(piece_multiplied, m - IN_FLIGHT + 1)
                span = slice(q * PK * TILE, (q + 1) * PK * TILE)
                nc.vector.tensor_tensor(tile_lo[:, m % IN_FLIGHT, :], tile(t, j)[:, span],
                                        tile_hi[:, m % IN_FLIGHT, :].bitcast(f32), ALU.subtract
                                        ).then_inc(lo_ready, 1)

            for i in range(NT):
                order = load_order(i)
                for pos in range(1, NT):
                    for j in (order[0:2] if pos == 1 else order[pos:pos + 1]):
                        wait_loaded(dve, i, j)
                    before = tile(i, order[0]) if pos == 1 else sums[:, :]
                    if i + pos > 1:
                        dve.wait_ge(added, adds_through(i, pos) - 1)
                    nc.vector.tensor_tensor(sums[:, :], before, tile(i, order[pos]), ALU.add).then_inc(added, 1)
                    if pos == 1 and i >= 1:
                        degree_guard(i - 1)
                dve.wait_ge(added, (i + 1) * ADDS - 2)
                nc.vector.tensor_tensor(sums[:, 0:2 * TILE], sums[:, 0:2 * TILE], sums[:, 2 * TILE:4 * TILE],
                                        ALU.add).then_inc(added, 1)
                dve.wait_ge(added, (i + 1) * ADDS - 1)
                if i >= 1:
                    dve.wait_ge(degree_product, i)
                nc.vector.tensor_tensor(folded[:, :], sums[:, 0:TILE], sums[:, TILE:2 * TILE], ALU.add
                                        ).then_inc(added, 1)
            degree_guard(NT - 1)

            def whole(e):
                t = FIRST_DONE + e
                wait_product(dve, *last_of[t])
                if e >= 2:
                    dve.wait_ge(turned_back, e - 1)
                if t < NT:
                    nc.vector.tensor_copy(whole_t[:, e % 2, :], acc[t % BANKS][:, :]
                                          ).then_inc(whole_ready, 1)
                else:
                    dve.wait_ge(park_loaded, 16 * (t - NT + 1))
                    nc.vector.tensor_tensor(whole_t[:, e % 2, :], acc[t % BANKS][:, :], park_in[:, :], ALU.add
                                            ).then_inc(whole_ready, 1)

            def residual(e):
                b, r = e % 2, row_of(FIRST_DONE + e)
                dve.wait_ge(xb_ready, e + 1)
                dve.wait_ge(turned_back, e + 1)
                if e >= 2:
                    dve.wait_ge(y_stored[b], 16 * (e // 2))
                for k in range(KB):
                    nc.vector.scalar_tensor_tensor(z[:, b, k, :], turned[b][:, k, :], d[:, r, k:k + 1],
                                                   x_in[:, b, k, :], ALU.mult, ALU.add,
                                                   accum_out=z_sum[:, b, k:k + 1]).then_inc(z_ready, 1)
                dve.wait_ge(z_ready, KB * (e + 1))
                nc.vector.tensor_scalar(minus_mean[:, b, :], z_sum[:, b, :], -1.0 / C, None, ALU.mult
                                        ).then_inc(mean_ready, 1)

            def deviation(e):
                b = e % 2
                dve.wait_ge(squared, KB * (e + 1))
                nc.vector.tensor_scalar(variance[:, b, :], square_sum[:, b, :], 1.0 / C, EPS,
                                        ALU.mult, ALU.add).then_inc(variance_ready, 1)

            def mean_shift(e):
                b = e % 2
                dve.wait_ge(rstd_ready, e + 1)
                nc.vector.tensor_tensor(shift[:, b, :], minus_mean[:, b, :], rstd[:, b, :], ALU.mult
                                        ).then_inc(shift_ready, 1)

            for n in range(split_no[FIRST_DONE, NT - 1], ROUNDS):
                if n < len(split_products):
                    t, j = split_products[n]
                    if brings_factor(t, j):
                        rest_of_factor(j)
                    for q in range(PIECES):
                        rest_of_piece(t, j, q)
                for step, do in ((WHOLE, whole), (RESIDUAL, residual), (VARIANCE, deviation),
                                 (SHIFT, mean_shift)):
                    for e in now(step, n):
                        do(e)

        @block.gpsimd
        def _(pool):
            nc.gpsimd.memset(ident[:, :], 0.0).then_inc(ident_cleared, 1)
            pool.wait_ge(ident_cleared, 1)
            nc.gpsimd.affine_select(out=ident[:, :], in_=ident[:, :], compare_op=ALU.not_equal, fill=1.0,
                                    base=0, pattern=[[-1, P]], channel_multiplier=1).then_inc(ident_ready, 1)
            pool.wait_ge(consts_set, 1)
            for i in range(NT):
                pool.wait_ge(degree_saved, i + 1)
                nc.gpsimd.tensor_tensor(d[:, i, :], degree[:, i, :], minus_half[:, :], ALU.pow
                                        ).then_inc(powered, 1)
            pool.wait_ge(bias_loaded, 16)
            for e in range(NT):
                pool.wait_ge(x_loaded[e % 2], 16 * (e // 2 + 1))
                nc.gpsimd.tensor_tensor(x_in[:, e % 2], x_in[:, e % 2],
                                        bias_in[:, None, :].to_broadcast([P, KB, C]), ALU.add
                                        ).then_inc(xb_ready, 1)
                pool.wait_ge(variance_ready, e + 1)
                nc.gpsimd.tensor_tensor(rstd[:, e % 2, :], variance[:, e % 2, :], minus_half[:, :], ALU.pow
                                        ).then_inc(rstd_ready, 1)

        @block.scalar
        def _(act):
            def round_factor(j):
                wait_factor_memory(act, j)
                act.wait_ge(scaled_ready, KB * (j + 1))
                nc.scalar.activation(factors[:, factor_no[j], 0], scaled[:, j * KB:(j + 1) * KB, :], ACT.Copy
                                     ).then_inc(factor_hi_ready, 1)

            def round_piece(t, j, q):
                m = PIECES * split_no[t, j] + q
                wait_loaded(act, t, j)
                if m >= IN_FLIGHT:
                    act.wait_ge(piece_multiplied, m - IN_FLIGHT + 1)
                span = slice(q * PK * TILE, (q + 1) * PK * TILE)
                nc.scalar.activation(tile_hi[:, m % IN_FLIGHT, :], tile(t, j)[:, span], ACT.Copy
                                     ).then_inc(hi_ready, 1)

            def load_rows(e):
                act.dma_start(x_in[:, e % 2], rows_of[row_of(FIRST_DONE + e)]).then_inc(x_loaded[e % 2], 16)

            for i in range(NT):
                act.wait_ge(xw_product, i + 1)
                nc.scalar.activation(scaled[:, i * KB:(i + 1) * KB, :], xw_ps[:, :, :], ACT.Copy
                                     ).then_inc(xw_saved, 1)
                act.wait_ge(degree_product, i + 1)
                nc.scalar.activation(degree[:, i, :], degree_ps[:, i % 2, :], ACT.Copy).then_inc(degree_saved, 1)
                act.wait_ge(d_ready, i + 1)
                act.wait_ge(xw_saved, i + 1)
                for k in range(KB):
                    nc.scalar.activation(scaled[:, i * KB + k, :], scaled[:, i * KB + k, :], ACT.Copy,
                                         scale=d[:, i, k:k + 1]).then_inc(scaled_ready, 1)
                for r in range(FIRST_DONE):
                    if last_of[r] == (r, i):
                        wait_product(act, r, i)
                        if r > 0:
                            act.wait_ge(park_stored, 16 * r)
                        nc.scalar.activation(park_out[:, :], acc[r % BANKS][:, :], ACT.Copy
                                             ).then_inc(park_ready, 1)
                        act.wait_ge(park_ready, r + 1)
                        act.dma_start(parked[r], park_out[:, :]).then_inc(park_stored, 16)
            act.wait_ge(xw_product, NT)
            act.dma_start(bias_in[:, :], bias.rearrange("(a c) -> a c", a=1).to_broadcast([P, C])
                          ).then_inc(bias_loaded, 16)
            act.wait_ge(degree_product, NT)
            load_rows(0)
            load_rows(1)

            def load_parked(t):
                if t == NT:
                    act.wait_ge(park_stored, 16 * PARKED)
                else:
                    act.wait_ge(whole_ready, t - FIRST_DONE)
                act.dma_start(park_in[:, :], parked[row_of(t)]).then_inc(park_loaded, 16)

            def squares_of(e):
                b = e % 2
                act.wait_ge(mean_ready, e + 1)
                for k in range(KB):
                    nc.scalar.activation(squares[:, k, :], z[:, b, k, :], ACT.Square,
                                         bias=minus_mean[:, b, k:k + 1],
                                         accum_out=square_sum[:, b, k:k + 1]).then_inc(squared, 1)
                if e + 2 < NT:
                    load_rows(e + 2)

            def store(e):
                b = e % 2
                act.wait_ge(squared, KB * (e + 1))
                act.wait_ge(shift_ready, e + 1)
                for k in range(KB):
                    nc.scalar.activation(z[:, b, k, :], z[:, b, k, :], ACT.Identity,
                                         bias=shift[:, b, k:k + 1], scale=rstd[:, b, k:k + 1]
                                         ).then_inc(y_ready, 1)
                act.wait_ge(y_ready, KB * (e + 1))
                act.dma_start(out_rows[row_of(FIRST_DONE + e)], z[:, b]).then_inc(y_stored[b], 16)

            load_parked(NT)
            for n in range(split_no[FIRST_DONE, NT - 1], ROUNDS):
                if n < len(split_products):
                    t, j = split_products[n]
                    if brings_factor(t, j):
                        round_factor(j)
                    for q in range(PIECES):
                        round_piece(t, j, q)
                for e in now(SQUARES, n):
                    squares_of(e)
                for e in now(STORE, n):
                    store(e)
                for e in now(WHOLE + 1, n):
                    if NT - FIRST_DONE <= e < NT - 1:
                        load_parked(FIRST_DONE + e + 1)
            for b in range(2):
                act.wait_ge(y_stored[b], 16 * (NT // 2))

        @block.tensor
        def _(pe):
            def xw(i):
                pe.wait_ge(xt_loaded, 16 * (i + 1))
                if i == 0:
                    pe.wait_ge(weight_loaded, 16)
                if i >= 1:
                    pe.wait_ge(xw_saved, i)
                for k in range(KB):
                    last = nc.tensor.matmul(xw_ps[:, k, :], xt_in[:, k * P:(k + 1) * P],
                                            w_in[:, :], start=True, stop=True)
                last.then_inc(xw_product, 1)

            def degrees(i):
                pe.wait_ge(added, (i + 1) * ADDS)
                if i == 0:
                    pe.wait_ge(consts_set, 1)
                if i >= 2:
                    pe.wait_ge(degree_saved, i - 1)
                for m in range(KB):
                    last = nc.tensor.matmul(degree_ps[:, i % 2, m:m + 1], folded[:, m * P:(m + 1) * P],
                                            ones[:, :], start=True, stop=True)
                last.then_inc(degree_product, 1)

            def multiply(t, j):
                first, last = (t, j) == first_of[t], (t, j) == last_of[t]
                if first and t >= BANKS:
                    before = t - BANKS
                    if before < FIRST_DONE:
                        pe.wait_ge(park_ready, before + 1)
                    else:
                        pe.wait_ge(whole_ready, before - FIRST_DONE + 1)
                if is_split(t, j):
                    multiply_split(t, j, first, last)
                    return
                wait_loaded(pe, t, j)
                pe.wait_ge(scaled_ready, KB * (j + 1))
                for k in range(KB):
                    mm = nc.tensor.matmul(acc[t % BANKS][:, :], scaled[:, j * KB + k, :],
                                          tile(t, j)[:, k * TILE:(k + 1) * TILE],
                                          start=(first and k == 0), stop=(last and k == KB - 1))
                mm.then_inc(multiplied, 1)

            def multiply_split(t, j, first, last):
                pe.wait_ge(factor_lo_ready, factor_no[j] + 1)
                bank = acc[t % BANKS][:, :]
                for q in range(PIECES):
                    m = PIECES * split_no[t, j] + q
                    pe.wait_ge(hi_ready, m + 1)
                    for k in range(PK):
                        hi, lo = (factors[:, factor_no[j], part, q * PK + k, :] for part in (0, 1))
                        moving = tile_hi[:, m % IN_FLIGHT, k * TILE:(k + 1) * TILE]
                        nc.tensor.matmul(bank, lo, moving, start=(first and q == 0 and k == 0), stop=False)
                        nc.tensor.matmul(bank, hi, moving, start=False, stop=False)
                    pe.wait_ge(lo_ready, m + 1)
                    for k in range(PK):
                        mm = nc.tensor.matmul(bank, factors[:, factor_no[j], 0, q * PK + k, :],
                                              tile_lo[:, m % IN_FLIGHT, k * TILE:(k + 1) * TILE],
                                              start=False, stop=(last and q == PIECES - 1 and k == PK - 1))
                    mm.then_inc(piece_multiplied, 1)

            def turn_back(e):
                pe.wait_ge(whole_ready, e + 1)
                if e >= 2:
                    pe.wait_ge(z_ready, KB * (e - 1))
                else:
                    pe.wait_ge(xw_saved, NT)
                if e == 0:
                    pe.wait_ge(ident_ready, 1)
                for k in range(KB):
                    last = nc.tensor.transpose(turned[e % 2][:, k, :], whole_t[:, e % 2, k * P:(k + 1) * P],
                                               ident[:, :])
                last.then_inc(turned_back, 1)

            for i in range(NT):
                xw(i)
                early = len(at_once(i)) - held_back(i)
                for j in at_once(i)[:early]:
                    multiply(i, j)
                degrees(i)
                for j in at_once(i)[early:]:
                    multiply(i, j)
                if i < NT - 1:
                    for k in waited_for(i):
                        multiply(k, i)
            for n in range(split_no[FIRST_DONE, NT - 1], ROUNDS):
                if n < len(split_products):
                    multiply(*split_products[n])
                for e in now(TURN_BACK, n):
                    turn_back(e)


def kernel(x, adj, L0_gnn_weight, L0_gnn_bias):
    import numpy as np
    import concourse.bacc as bacc
    from concourse import mybir
    from concourse.bass_utils import run_bass_kernel_spmd

    tile, part = 512, 128
    n, c = x.shape
    nt, kb = n // tile, tile // part
    adj = np.asarray(adj)
    x = np.ascontiguousarray(x)
    adj_t = np.ascontiguousarray(
        adj.reshape(nt, tile, nt, kb, part).transpose(0, 2, 4, 3, 1)).reshape(nt, nt, part, kb * tile)
    arrays = {
        "adj_t": adj_t, "x": x, "x_t": np.ascontiguousarray(x.T),
        "weight": np.ascontiguousarray(L0_gnn_weight), "bias": np.ascontiguousarray(L0_gnn_bias),
    }
    nc = bacc.Bacc("TRN2", target_bir_lowering=False, num_devices=1)
    aps = {name: nc.dram_tensor(name, a.shape, mybir.dt.from_np(a.dtype), kind="ExternalInput").ap()
           for name, a in arrays.items()}
    aps["adj_t"] = aps["adj_t"].rearrange("i j p (k r) -> i j p k r", k=kb)
    parked = nc.dram_tensor("parked", (nt, part, tile), mybir.dt.float32, kind="Internal").ap()
    out = nc.dram_tensor("out", (n, c), mybir.dt.float32, kind="ExternalOutput").ap()
    normalized_adjacency_layernorm(nc, aps["adj_t"], aps["x"], aps["x_t"], aps["weight"], aps["bias"], parked, out)
    result = run_bass_kernel_spmd(nc, [arrays], core_ids=[0])
    return result.results[0]["out"]
```
